# Optimizing a Trainium2 kernel written in Bass

```python
import numpy as np
import jax
import jax.numpy as jnp

def _softmax(x, axis=-1):
    return jax.nn.softmax(x, axis=axis)

def _gelu(x):
    return jax.nn.gelu(x, approximate=True)

def _silu(x):
    return jax.nn.silu(x)

def _sigmoid(x):
    return jax.nn.sigmoid(x)

def _layernorm(x, axis=-1, eps=1e-05):
    m = jnp.mean(x, axis=axis, keepdims=True)
    v = jnp.var(x, axis=axis, keepdims=True)
    return (x - m) / jnp.sqrt(v + eps)

def _scatter_add(tgt, idx, src, axis=0):
    return tgt.at[idx].add(src)

def _segment_sum(src, seg, n):
    return jax.ops.segment_sum(src, seg, n)
kernel_name = 'mk_decoder_postln_d1_seqx_r4_b427f4'

def setup_inputs(seed: int=0):
    np.random.seed(seed)
    _w = jnp.asarray

    def _rec_inputs():
        import jax
        import jax.numpy as jnp
        _rk = jax.random.key(seed)
        x = 7.22e-05 + 1 * jax.random.normal(jax.random.fold_in(_rk, 1), (64, 128, 256), jnp.float32)
        _lenS = 128 - jax.random.randint(jax.random.fold_in(_rk, 7), (64,), 0, max(1, 128 // 4) + 1, jnp.int32)
        _lenS2 = 128 - jax.random.randint(jax.random.fold_in(_rk, 8), (64,), 0, max(1, 128 // 4) + 1, jnp.int32)
        _ctx_1024P = jax.random.normal(jax.random.fold_in(_rk, 11), (64, 16, 256), jnp.float32)
        _ctx_1024c = jax.random.dirichlet(jax.random.fold_in(_rk, 511), 0.3 * jnp.ones((16,), jnp.float32), (64, 128))
        _ctx_1024t = jnp.einsum('bsk,bkd->bsd', _ctx_1024c, _ctx_1024P)
        _ctx_1024t = _ctx_1024t * jax.lax.rsqrt(jnp.mean(jnp.square(_ctx_1024t)) + 1e-12) * 0.953939
        ctx_1024 = -0.000514642 + 1.00011 * (_ctx_1024t + 0.3 * jax.random.normal(jax.random.fold_in(_rk, 611), (64, 128, 256), jnp.float32))
        return (x, ctx_1024)
    x, ctx_1024 = _rec_inputs()

    def _L0_attn_setup():
        import jax, jax.numpy as jnp
        import numpy as np
        import math
        B_SZ, L, D, S = (4, 1024, 256, 64)

        def _blelloch_exclusive_scan(a, b):

            def combine(p, q):
                pa, pb = p
                qa, qb = q
                return (pa * qa, pa * qb + pb)
            _, b_inc = jax.lax.associative_scan(combine, (a, b), axis=1)
            return jnp.concatenate([jnp.zeros_like(b_inc[:, :1]), b_inc[:, :-1]], axis=1)
        key = jax.random.key(seed)
        k0, k1, k2, k3 = jax.random.split(key, 4)
        x = jax.random.normal(k0, (B_SZ, L, D), dtype=jnp.float32)
        B_w = jax.random.normal(k1, (S, D), dtype=jnp.float32) * (1.0 / math.sqrt(D))
        C_w = jax.random.normal(k2, (D, S), dtype=jnp.float32) * (1.0 / math.sqrt(S))
        gate_w = jax.random.normal(k3, (D, D), dtype=jnp.float32) * (1.0 / math.sqrt(D))
        gate_b = jnp.zeros((D,), dtype=jnp.float32)
        log_decay = jnp.full((D,), math.log(0.9), dtype=jnp.float32)
        return {'x': x, 'B_w': B_w, 'C_w': C_w, 'gate_w': gate_w, 'gate_b': gate_b, 'log_decay': log_decay}
    _L0_attn_all = _L0_attn_setup()
    _L0_attn_in = {k: v for k, v in _L0_attn_all.items() if k in ('B_w', 'C_w', 'gate_w', 'gate_b', 'log_decay')}
    del _L0_attn_all

    def _L0_xattn_setup():
        import jax, jax.numpy as jnp
        import numpy as np
        B, L_ENC, L_DEC, D = (16, 128, 128, 256)
        key = jax.random.key(seed)
        k1, k2, k3, k4, k5, k6 = jax.random.split(key, 6)
        encoder_hc = jax.random.normal(k1, (B, L_ENC, D), dtype=jnp.float32)
        decoder_hq = jax.random.normal(k2, (B, L_DEC, D), dtype=jnp.float32)
        w_sim = jax.random.normal(k3, (3 * D,), dtype=jnp.float32) * 0.02
        b_sim = jax.random.normal(k4, (1,), dtype=jnp.float32) * 0.02
        W_qv = jax.random.normal(k5, (4 * D, D), dtype=jnp.float32) * 0.02
        b_qv = jax.random.normal(k6, (D,), dtype=jnp.float32) * 0.02
        return {'encoder_hc': encoder_hc, 'decoder_hq': decoder_hq, 'w_sim': w_sim, 'b_sim': b_sim, 'W_qv': W_qv, 'b_qv': b_qv}
    _L0_xattn_all = _L0_xattn_setup()
    _L0_xattn_in = {k: v for k, v in _L0_xattn_all.items() if k in ('w_sim', 'b_sim', 'W_qv', 'b_qv')}
    del _L0_xattn_all

    def _L0_ffn_setup():
        import jax, jax.numpy as jnp
        import numpy as np
        D, H, E, K, S = (256, 512, 8, 2, 1)
        B, L = (4, 512)
        key = jax.random.key(seed)
        ks = jax.random.split(key, 9)
        std = 0.02
        return {'x': jax.random.normal(ks[0], (B, L, D), dtype=jnp.float32), 'router_w': jax.random.normal(ks[1], (E, D), dtype=jnp.float32) * std, 'experts_bias': jnp.zeros((E,), dtype=jnp.float32), 'w1': jax.random.normal(ks[2], (E, D, H), dtype=jnp.float32) * std, 'w3': jax.random.normal(ks[3], (E, D, H), dtype=jnp.float32) * std, 'w2': jax.random.normal(ks[4], (E, H, D), dtype=jnp.float32) * std, 'sw1': jax.random.normal(ks[5], (S, D, H), dtype=jnp.float32) * std, 'sw3': jax.random.normal(ks[6], (S, D, H), dtype=jnp.float32) * std, 'sw2': jax.random.normal(ks[7], (S, H, D), dtype=jnp.float32) * std}
    _L0_ffn_all = _L0_ffn_setup()
    _L0_ffn_in = {k: v for k, v in _L0_ffn_all.items() if k in ('router_w', 'experts_bias', 'w1', 'w3', 'w2', 'sw1', 'sw3', 'sw2')}
    del _L0_ffn_all
    return {'x': x, 'ctx_1024': ctx_1024, 'L0_attn_B_w': _L0_attn_in['B_w'], 'L0_attn_C_w': _L0_attn_in['C_w'], 'L0_attn_gate_w': _L0_attn_in['gate_w'], 'L0_attn_gate_b': _L0_attn_in['gate_b'], 'L0_attn_log_decay': _L0_attn_in['log_decay'], 'L0_xattn_w_sim': _L0_xattn_in['w_sim'], 'L0_xattn_b_sim': _L0_xattn_in['b_sim'], 'L0_xattn_W_qv': _L0_xattn_in['W_qv'], 'L0_xattn_b_qv': _L0_xattn_in['b_qv'], 'L0_ffn_router_w': _L0_ffn_in['router_w'], 'L0_ffn_experts_bias': _L0_ffn_in['experts_bias'], 'L0_ffn_w1': _L0_ffn_in['w1'], 'L0_ffn_w3': _L0_ffn_in['w3'], 'L0_ffn_w2': _L0_ffn_in['w2'], 'L0_ffn_sw1': _L0_ffn_in['sw1'], 'L0_ffn_sw3': _L0_ffn_in['sw3'], 'L0_ffn_sw2': _L0_ffn_in['sw2']}

def reference(x, ctx_1024, L0_attn_B_w, L0_attn_C_w, L0_attn_gate_w, L0_attn_gate_b, L0_attn_log_decay, L0_xattn_w_sim, L0_xattn_b_sim, L0_xattn_W_qv, L0_xattn_b_qv, L0_ffn_router_w, L0_ffn_experts_bias, L0_ffn_w1, L0_ffn_w3, L0_ffn_w2, L0_ffn_sw1, L0_ffn_sw3, L0_ffn_sw2):
    import jax
    import jax.numpy as jnp

    def _L0_attn_ref(x, B_w, C_w, gate_w, gate_b, log_decay):
        import jax, jax.numpy as jnp
        import numpy as np
        import math
        B_SZ, L, D, S = (4, 1024, 256, 64)

        def _blelloch_exclusive_scan(a, b):

            def combine(p, q):
                pa, pb = p
                qa, qb = q
                return (pa * qa, pa * qb + pb)
            _, b_inc = jax.lax.associative_scan(combine, (a, b), axis=1)
            return jnp.concatenate([jnp.zeros_like(b_inc[:, :1]), b_inc[:, :-1]], axis=1)
        Bu = jnp.einsum('bld,sd->bls', x, B_w)
        Bu_proj = jnp.einsum('bls,ds->bld', Bu, C_w)
        decay = jax.nn.sigmoid(log_decay)
        a = jnp.broadcast_to(decay, Bu_proj.shape)
        h = _blelloch_exclusive_scan(a, Bu_proj)
        gate = jax.nn.sigmoid(jnp.einsum('bld,ed->ble', x, gate_w) + gate_b)
        return gate * h

    def _L0_xattn_ref(encoder_hc, decoder_hq, w_sim, b_sim, W_qv, b_qv):
        import jax, jax.numpy as jnp
        import numpy as np
        B, L_ENC, L_DEC, D = (16, 128, 128, 256)
        d = encoder_hc.shape[-1]
        w1, w2, w3 = (w_sim[:d], w_sim[d:2 * d], w_sim[2 * d:])
        Sim = (encoder_hc @ w1)[:, :, None] + (decoder_hq @ w2)[:, None, :] + jnp.einsum('bid,bjd->bij', encoder_hc * w3, decoder_hq) + b_sim[0]
        A = jax.nn.softmax(Sim, axis=2)
        hq_hat = jnp.einsum('bij,bjd->bid', A, decoder_hq)
        Batt = jax.nn.softmax(jnp.max(Sim, axis=2), axis=1)
        hc_bar = jnp.einsum('bi,bid->bd', Batt, encoder_hc)[:, None, :]
        hc_hat = jnp.broadcast_to(hc_bar, encoder_hc.shape)
        feats = jnp.concatenate([encoder_hc, hq_hat, encoder_hc * hq_hat, encoder_hc * hc_hat], axis=-1)
        hcq = feats @ W_qv + b_qv
        return hcq

    def _L0_ffn_ref(x, router_w, experts_bias, w1, w3, w2, sw1, sw3, sw2):
        import jax, jax.numpy as jnp
        import numpy as np
        D, H, E, K, S = (256, 512, 8, 2, 1)
        B, L = (4, 512)
        b, l, d = x.shape
        xf = x.reshape(-1, d)
        sg = jnp.einsum('td,sdh->tsh', xf, sw1)
        su = jnp.einsum('td,sdh->tsh', xf, sw3)
        shared_out = jnp.einsum('tsh,shd->td', jax.nn.silu(sg) * su, sw2)
        logits = xf @ router_w.T + experts_bias
        rw, sel = jax.lax.top_k(logits, K)
        rw = jax.nn.softmax(rw.astype(jnp.float32), axis=-1).astype(x.dtype)
        cw = (jax.nn.one_hot(sel, E, dtype=x.dtype) * rw[..., None]).sum(axis=1)
        g = jnp.einsum('td,edh->teh', xf, w1)
        u = jnp.einsum('td,edh->teh', xf, w3)
        eo = jax.nn.silu(g) * u
        moe_out = jnp.einsum('te,teh,ehd->td', cw, eo, w2)
        return (moe_out + shared_out).reshape(b, l, d)
    x = _layernorm(x + _L0_attn_ref(x, L0_attn_B_w, L0_attn_C_w, L0_attn_gate_w, L0_attn_gate_b, L0_attn_log_decay), axis=-1)
    x = _layernorm(x + _L0_xattn_ref(x, ctx_1024, L0_xattn_w_sim, L0_xattn_b_sim, L0_xattn_W_qv, L0_xattn_b_qv), axis=-1)
    x = _layernorm(x + _L0_ffn_ref(x, L0_ffn_router_w, L0_ffn_experts_bias, L0_ffn_w1, L0_ffn_w3, L0_ffn_w2, L0_ffn_sw1, L0_ffn_sw3, L0_ffn_sw2), axis=-1)
    return x

_drawn_inputs = setup_inputs


def setup_inputs(seed=0):
    import zlib

    import numpy as np

    out = dict(_drawn_inputs(seed))
    spreads = {'L0_attn_gate_b': (0.0, 0.342),
     'L0_attn_log_decay': (-0.10536051541566849, 0.6),
     'L0_ffn_experts_bias': (0.0, 0.8)}
    factors = {'L0_xattn_b_qv': 2.94,
     'L0_ffn_router_w': 3.902,
     'L0_ffn_w1': 3.353,
     'L0_ffn_w3': 3.316,
     'L0_ffn_w2': 3.319,
     'L0_ffn_sw1': 3.053,
     'L0_ffn_sw3': 3.001,
     'L0_ffn_sw2': 3.023}
    for name, (base, spread) in spreads.items():
        noise = np.random.default_rng([zlib.crc32(name.encode()), seed]).standard_normal(out[name].shape)
        drawn = base * np.exp(spread * noise) if base else spread * noise
        out[name] = jnp.asarray(drawn.astype(out[name].dtype))
    for name, factor in factors.items():
        out[name] = (out[name] * factor).astype(out[name].dtype)
    return out
```

```python
from contextlib import ExitStack

import numpy as np

import concourse.bass as bass
from concourse import mybir

F32 = mybir.dt.float32
BF16 = mybir.dt.bfloat16
U32 = mybir.dt.uint32
I32 = mybir.dt.int32
ALU = mybir.AluOpType
ACT = mybir.ActivationFunctionType
AX_X = mybir.AxisListType.X

P = 128
NSEQ, L, D = 64, 128, 256
S, H, E, TOPK = 64, 512, 8, 2
DC, HC = D // P, H // P
EPS = 1e-5
UNROLL = 4
REGION = NSEQ * L + P
NTILES = NSEQ * L * TOPK // P + E
SPARE = E
ROWS = E * REGION + SPARE * P


class Seq:

    def __init__(self, j, off, total=NSEQ):
        self.j, self.off, self.n = j, off, j * UNROLL + off
        self.real = not isinstance(j, int) or 0 <= self.n < total

    def slot(self, ring):
        return self.off % ring

    def turn(self, ring):
        return self.j * (UNROLL // ring) + self.off // ring


def build(nc, x, ctxt, BwT, CwT, gwT, gate_b, log_decay, w_sim, b_sim, W_qv, b_qv, rwT, ebias,
          w1, w3, w2, sw1, sw3, sw2, c_ident, c_tri, c_iota8, c_iotap, c_jrow, c_ereg, out, xs, ys):
    with ExitStack() as stack:
        def sb(name, shape, dt=F32):
            return stack.enter_context(nc.sbuf_tensor(name, shape, dt))

        def sem(name):
            return stack.enter_context(nc.semaphore(name))

        bank = [stack.enter_context(nc.psum_tensor(f"bank{i}", [P, 512], F32)) for i in range(8)]
        xT_ps = bank[0][:, :]
        x2T_ps = bank[0][:, 0:D]
        x1T_ps = bank[1][:, 0:D]
        bp_ps = bank[1][:, 0:D]
        pb_ps = bank[1][:, 0:P]
        y_ps = bank[2][:, 0:D]
        hqT_ps = bank[2][:, 0:D]
        sim_ps = bank[3][:, 0:P]
        s_ps = bank[3][:, P:P + 1]
        lg_ps = bank[3][:, 2 * P:2 * P + E]
        rank_ps = bank[3][:, 3 * P:3 * P + E]
        total_ps = bank[3][:, 3 * P + E:3 * P + 2 * E]
        bu_ps = bank[4][0:S, 0:P]
        gate_ps = bank[4][:, P:P + D]
        aT_ps = bank[4][:, 0:P]
        vrow_ps = bank[4][0:1, P:2 * P]
        cum_ps = bank[4][:, 0:D]
        g_ps = bank[5][:, :]
        thT_ps = bank[1][:, :]
        u_ps = bank[6][:, :]
        qv_ps = bank[7][:, 0:D]

        w13_sb = sb("w13_sb", [P, E, DC, 2 * H])
        w2_sb = sb("w2_sb", [P, E, HC, D])
        gwT_sb = sb("gwT_sb", [P, DC, D])
        BwT_sb = sb("BwT_sb", [P, DC, S])
        CwT_sb = sb("CwT_sb", [S, D])
        Wqv_sb = sb("Wqv_sb", [P, 4 * DC, D])
        rwT_sb = sb("rwT_sb", [P, DC, E])
        wsim_sb = sb("wsim_sb", [P, 3, DC])
        bsim_sb = sb("bsim_sb", [P, 1])
        gb_sb = sb("gb_sb", [1, D])
        bqv_sb = sb("bqv_sb", [1, D])
        ebias_sb = sb("ebias_sb", [P, E])
        ident = sb("ident", [P, P])
        tri = sb("tri", [P, P])
        tri_b = sb("tri_b", [P, P], BF16)
        ones_b = sb("ones_b", [P, P], BF16)
        ones_row = sb("ones_row", [1, P])
        iota8 = sb("iota8", [P, E])
        iotap = sb("iotap", [P, 1])
        mhalf = sb("mhalf", [P, 1])
        eps = sb("eps", [P, 1])
        decay = sb("decay", [P, 3, DC])
        apow = sb("apow", [P, D])

        base = sb("base", [P, NSEQ, D])
        top2 = sb("top2", [P, NSEQ, TOPK])
        posall = sb("posall", [P, NSEQ, TOPK])
        count = sb("count", [P, E])
        padidx = sb("padidx", [P, E], U32)

        x_sb = sb("x_sb", [P, 2, D])
        c_sb = sb("c_sb", [P, 2, D])
        xcT = sb("xcT", [P, 2, 2 * DC, P])
        buT = sb("buT", [S, P])
        th = sb("th", [P, D])
        bpw = sb("bpw", [P, D])
        x1 = sb("x1", [P, 2, D])
        x1T = sb("x1T", [P, DC, P])
        qT = sb("qT", [P, DC, P])
        aexp = sb("aexp", [P, P])
        aT = sb("aT", [P, P])
        hqT = sb("hqT", [P, DC, P])
        x1hqT = sb("x1hqT", [P, DC, P])
        x1hcT = sb("x1hcT", [P, DC, P])
        apowT = x1hcT[:, :, :]
        zeros = bpw[:, :]
        x2 = sb("x2", [P, 2, D])
        x2T = sb("x2T", [P, DC, P])
        thg = sb("thg", [P, H])
        hT = sb("hT", [P, HC, P])
        bn1 = sb("bn1", [P, 6])
        mv1 = sb("mv1", [P, 2])
        ve1 = sb("ve1", [P, 1])
        rs1 = sb("rs1", [P, 1])
        bn2 = sb("bn2", [P, 6])
        mv2 = sb("mv2", [P, 2])
        ve2 = sb("ve2", [P, 1])
        rs2 = sb("rs2", [P, 1])
        smax = sb("smax", [P, 2])
        rsum = sb("rsum", [P, 2])
        vcol = sb("vcol", [P, 1])
        vst = sb("vst", [1, 4])
        vrow = sb("vrow", [1, P])
        vprob = sb("vprob", [1, P])
        hc = sb("hc", [P, DC])
        junk8 = sb("junk8", [P, TOPK, E])
        lg = sb("lg", [P, E])
        m8 = sb("m8", [P, 8])
        i8 = sb("i8", [P, 8], U32)
        idxf = sb("idxf", [P, TOPK])
        oh = sb("oh", [P, TOPK, E])
        ohb = sb("ohb", [P, E], BF16)
        place = sb("place", [P, E])
        posf = sb("posf", [P, TOPK])
        posr = sb("posr", [P, UNROLL, TOPK], U32)

        jrow = sb("jrow", [1, NTILES])
        ereg = sb("ereg", [P, E])
        cnt1 = sb("cnt1", [P, E])
        cnti = sb("cnti", [P, E], I32)
        cntsh = sb("cntsh", [P, E], I32)
        ntile = sb("ntile", [P, E])
        tend = sb("tend", [P, E])
        skip = sb("skip", [P, E])
        tacc = c_sb[0:1, :, :].rearrange("p a d -> p (a d)")[:, 0:3 * NTILES].rearrange("p (a n) -> p a n", a=3)
        tile_e = sb("tile_e", [1, NTILES], I32)
        tile_row = sb("tile_row", [1, NTILES], I32)

        const_in = sem("const_in")
        moe_in = sem("moe_in")
        last_in = sem("last_in")
        x_in = [sem(f"x_in{i}") for i in range(2)]
        c_in = [sem(f"c_in{i}") for i in range(2)]
        setup = sem("setup")
        pow_ready = sem("pow_ready")
        apow_ps_ready = sem("apow_ps_ready")
        apow_ready = sem("apow_ready")
        consts_ready = sem("consts_ready")
        xT_mm, gate_mm, bp_mm, cum_mm, x1T_mm, sim_mm, aT_mm, hq_mm, pb_mm, qv_mm, x2T_mm, lg_mm, \
            g_mm, u_mm, rank_mm, y_mm = [sem(n) for n in (
                "xT_mm gate_mm bp_mm cum_mm x1T_mm sim_mm aT_mm hq_mm pb_mm qv_mm x2T_mm lg_mm "
                "g_mm u_mm rank_mm y_mm").split()]
        xcT_sb, buT_sb, th_sb, x1T_sb, aexp_sb, aT_sb, vexp_sb, hqT_sb, x2T_sb, thg_sb = [sem(n) for n in (
            "xcT_sb buT_sb th_sb x1T_sb aexp_sb aT_sb vexp_sb hqT_sb x2T_sb thg_sb").split()]
        qT_sb, bpw_sb, gated, res1, st1, mv1_s, x1_sb, res2, st2, mv2_s, x2_sb = [sem(n) for n in (
            "qT_sb bpw_sb gated res1 st1 mv1_s x1_sb res2 st2 mv2_s x2_sb").split()]
        smax_s, nmax_s, v_s, rec_s, anorm_s, vmax_s, nvmax_s, vrec_s, vprob_s, hc_s, x1hq_s, x1hc_s = [sem(n) for n in (
            "smax_s nmax_s v_s rec_s anorm_s vmax_s nvmax_s vrec_s vprob_s hc_s x1hq_s x1hc_s").split()]
        lg_s, m8_s, i8_s, idx_s, oh_s, ohb_s, place_s, posf_s, count_s, pos_s, hg_s, hT_s, base_s = [sem(n) for n in (
            "lg_s m8_s i8_s idx_s oh_s ohb_s place_s posf_s count_s pos_s hg_s hT_s base_s").split()]
        ve1_s, rs1_s, ve2_s, rs2_s = [sem(n) for n in "ve1_s rs1_s ve2_s rs2_s".split()]
        row_out = [sem(f"row_out{i}") for i in range(2)]
        spare_out = sem("spare_out")
        pad_out = sem("pad_out")
        pad_ready = sem("pad_ready")
        pos_final = sem("pos_final")
        zero_ready = sem("zero_ready")
        table = sem("table")
        table_ready = sem("table_ready")
        wexp_s = sem("wexp_s")
        wt_s = sem("wt_s")
        t_in = [sem(f"t_in{i}") for i in range(2)]
        t_out = [sem(f"t_out{i}") for i in range(2)]
        tT_mm, tT_sb, tg_mm, tu_mm, tth_s, thg_s, th_s, thT_mm, thT_sb, ty_mm, ty_sb = [sem(n) for n in (
            "tT_mm tT_sb tg_mm tu_mm tth_s thg_s th_s thT_mm thT_sb ty_mm ty_sb").split()]
        gidx_s = sem("gidx_s")
        ya_in = [sem(f"ya_in{i}") for i in range(2)]
        yb_in = [sem(f"yb_in{i}") for i in range(2)]
        acc_s, res3, st3, mv3_s, ve3_s, rs3_s, out_s = [sem(n) for n in "acc_s res3 st3 mv3_s ve3_s rs3_s out_s".split()]
        out_done = [sem(f"out_done{i}") for i in range(2)]

        NCONST = 18

        def wait(eng, s, count):
            if not isinstance(count, int) or count > 0:
                eng.wait_ge(s, count)

        def wait_alone(eng, s, count):
            if not isinstance(count, int):
                eng.wait_ge(const_in, 16)
            wait(eng, s, count)

        def pipeline(eng, step, total, lead, depth):
            for s in range(lead):
                step(s // UNROLL, s % UNROLL)
            with eng.Fori(lead // UNROLL, total // UNROLL, 1) as j:
                for off in range(UNROLL):
                    step(j, off)
            for s in range(total, total + depth):
                step(s // UNROLL, s % UNROLL)

        def upto(t, k):
            return min(t.n + k, NSEQ) if isinstance(t.n, int) else t.n + k

        def run_pass1(eng, step):
            pipeline(eng, step, NSEQ, 2 * UNROLL, 3)

        block = stack.enter_context(nc.Block())

        @block.sync
        def _(sp):
            for dst, src in [
                    (ident[:, :], c_ident), (BwT_sb[:, :, :], BwT.rearrange("(c p) s -> p c s", p=P)),
                    (gwT_sb[:, :, :], gwT.rearrange("(c p) s -> p c s", p=P)), (gb_sb[:, :], gate_b),
                    (decay[:, 0, :], log_decay), (CwT_sb[:, :], CwT), (tri[:, :], c_tri),
                    (wsim_sb[:, :, :], w_sim), (bsim_sb[:, :], b_sim.partition_broadcast(P)),
                    (iota8[:, :], c_iota8), (iotap[:, :], c_iotap), (jrow[:, :], c_jrow), (ereg[:, :], c_ereg.partition_broadcast(P)),
                    (Wqv_sb[:, :, :], W_qv.rearrange("(c p) n -> p c n", p=P)), (bqv_sb[:, :], b_qv),
                    (rwT_sb[:, :, :], rwT.rearrange("(c p) e -> p c e", p=P)),
                    (ebias_sb[:, :], ebias.partition_broadcast(P)),
                    (count[:, :], c_ereg.partition_broadcast(P))]:
                sp.dma_start(dst, src).then_inc(const_in, 16)

            def load(j, off):
                t = Seq(j, off)
                wait(sp, res1, t.n - 1)
                sp.dma_start(x_sb[:, t.slot(2), :], x[bass.ds(t.n, 1), :, :].rearrange("a l d -> (a l) d")) \
                    .then_inc(x_in[t.slot(2)], 16)
                wait(sp, hq_mm, t.n - 1)
                sp.dma_start(c_sb[:, t.slot(2), :], ctxt[bass.ds(t.n, 1), :, :].rearrange("a l d -> (a l) d")) \
                    .then_inc(c_in[t.slot(2)], 16)

            load(0, 0)
            for dst, src in [(w13_sb[:, E - 1, :, 0:H], sw1), (w13_sb[:, E - 1, :, H:], sw3), (w2_sb[:, E - 1, :, :], sw2)]:
                sp.dma_start(dst, src.rearrange("(c p) n -> p c n", p=P)).then_inc(last_in, 16)
            for s in range(1, UNROLL):
                load(0, s)
            with sp.Fori(1, NSEQ // UNROLL, 1) as j:
                for off in range(UNROLL):
                    load(j, off)
            sp.wait_ge(y_mm, NSEQ)
            for dst, src in [(w13_sb[:, E - 1, :, 0:H], w1[E - 1]), (w13_sb[:, E - 1, :, H:], w3[E - 1]),
                             (w2_sb[:, E - 1, :, :], w2[E - 1])]:
                sp.dma_start(dst, src.rearrange("(c p) n -> p c n", p=P)).then_inc(last_in, 16)

            sp.wait_ge(table_ready, 1)
            for i in range(2):
                sp.wait_ge(row_out[i], 2 * 16 * NSEQ // 2)
            sp.wait_ge(pad_out, 16 * E)
            sp.wait_ge(spare_out, 16 * SPARE)

            def tiles(j, off):
                t, o = Seq(j, off, NTILES), Seq(j, off - 2, NTILES)
                if t.real:
                    row = sp.value_load(tile_row[0:1, bass.ds(t.n, 1)], min_val=0, max_val=ROWS - P)
                    wait(sp, tT_mm, t.n - 1)
                    sp.dma_start(x_sb[:, t.slot(2), :], xs[bass.ds(row, P), :]).then_inc(t_in[t.slot(2)], 16)
                if o.real:
                    wait(sp, ty_sb, o.n + 1)
                    sp.dma_start(ys[bass.ds(o.n, 1), :, :].rearrange("a p d -> (a p) d"), c_sb[:, o.slot(2), :]).then_inc(t_out[o.slot(2)], 16)
            pipeline(sp, tiles, NTILES, UNROLL, 2)

            def store(j, off):
                t = Seq(j, off)
                sp.wait_ge(out_s, t.n + 1)
                sp.dma_start(out[bass.ds(t.n, 1), :, :].rearrange("a l d -> (a l) d"), x2[:, t.slot(2), :]) \
                    .then_inc(out_done[t.slot(2)], 16)
            with sp.Fori(0, NSEQ // UNROLL, 1) as j:
                for off in range(UNROLL):
                    store(j, off)
            for i in range(2):
                sp.wait_ge(out_done[i], 16 * NSEQ // 2)

        @block.gpsimd
        def _(pool):
            nc.gpsimd.memset(ones_b[:, :], 1.0).then_inc(consts_ready, 1)
            nc.gpsimd.memset(ones_row[:, :], 1.0).then_inc(consts_ready, 1)
            nc.gpsimd.memset(eps[:, :], EPS).then_inc(consts_ready, 1)
            nc.gpsimd.memset(mhalf[:, :], -0.5).then_inc(consts_ready, 1)
            pool.wait_ge(consts_ready, 4)
            pool.wait_ge(last_in, 48)
            for e in range(E - 1):
                for dst, src in [(w13_sb[:, e, :, 0:H], w1[e]), (w13_sb[:, e, :, H:], w3[e]), (w2_sb[:, e, :, :], w2[e])]:
                    pool.dma_start(dst, src.rearrange("(c p) n -> p c n", p=P)).then_inc(moe_in, 16)

            def norm(t, mv, mv_s, ve, ve_s, rs, rs_s, used):
                pool.wait_ge(mv_s, t.n + 1)
                nc.gpsimd.tensor_tensor(ve[:, :], mv[:, 1:2], eps[:, :], ALU.add).then_inc(ve_s, 1)
                pool.wait_ge(ve_s, t.n + 1)
                wait(pool, used, t.n)
                nc.gpsimd.tensor_tensor(rs[:, :], ve[:, :], mhalf[:, :], ALU.pow).then_inc(rs_s, 1)

            def step(j, off):
                a, b, c = Seq(j, off), Seq(j, off - 2), Seq(j, off - 2)
                if b.real:
                    norm(b, mv2, mv2_s, ve2, ve2_s, rs2, rs2_s, x2_sb)
                if a.real:
                    norm(a, mv1, mv1_s, ve1, ve1_s, rs1, rs1_s, x1_sb)
                if c.real:
                    wait_alone(pool, x2_sb, c.n + 1)
                    pool.wait_ge(pos_s, c.n + 1)
                    for k in range(TOPK):
                        pool.indirect_dma_start(
                            out=xs[:, :], out_offset=bass.IndirectOffsetOnAxis(ap=posr[:, c.slot(UNROLL), k:k + 1], axis=0),
                            in_=x2[:, c.slot(2), :], in_offset=None).then_inc(row_out[c.slot(2)], 16)
            run_pass1(pool, step)

            pool.wait_ge(cum_mm, NSEQ)
            nc.gpsimd.memset(zeros, 0.0).then_inc(zero_ready, 1)
            pool.wait_ge(zero_ready, 1)
            for i in range(SPARE):
                pool.dma_start(xs[E * REGION + i * P:E * REGION + (i + 1) * P, :], zeros).then_inc(spare_out, 16)
            pool.wait_ge(pad_ready, 1)
            for e in range(E):
                pool.indirect_dma_start(
                    out=xs[:, :], out_offset=bass.IndirectOffsetOnAxis(ap=padidx[:, e:e + 1], axis=0),
                    in_=zeros, in_offset=None).then_inc(pad_out, 16)

            for i in range(2):
                pool.wait_ge(t_out[i], 16 * NTILES // 2)
            pool.wait_ge(pos_final, 1)

            def gather(j, off):
                t, b = Seq(j, off), Seq(j, off - 1)
                if t.real:
                    wait(pool, res3, t.n - 1)
                    pool.wait_ge(pos_s, t.n + 1)
                    nc.gpsimd.tensor_copy(posr[:, t.slot(UNROLL), :],
                                          posall[:, bass.ds(t.n, 1), :].rearrange("p a k -> p (a k)")).then_inc(gidx_s, 1)
                    wait_alone(pool, gidx_s, t.n + 1)
                    for k, (dst, s) in enumerate([(x_sb, ya_in), (c_sb, yb_in)]):
                        pool.indirect_dma_start(
                            out=dst[:, t.slot(2), :], out_offset=None, in_=ys.rearrange("a p d -> (a p) d"),
                            in_offset=bass.IndirectOffsetOnAxis(ap=posr[:, t.slot(UNROLL), k:k + 1], axis=0)) \
                            .then_inc(s[t.slot(2)], 16)
                if b.real:
                    norm(b, mv1, mv3_s, ve1, ve3_s, rs1, rs3_s, out_s)
            pipeline(pool, gather, NSEQ, UNROLL, 1)

        @block.scalar
        def _(act):
            act.wait_ge(const_in, 16 * NCONST)
            nc.scalar.activation(decay[:, 1, :], decay[:, 0, :], ACT.Exp, scale=-1.0).then_inc(setup, 1)

            def step(j, off):
                a, b, c = Seq(j, off), Seq(j, off - 1), Seq(j, off - 2)
                if b.real:
                    act.wait_ge(x1T_mm, b.n + 1)
                    nc.scalar.copy(x1T[:, :, :].rearrange("p c t -> p (c t)"), x1T_ps).then_inc(x1T_sb, 1)
                if a.real:
                    act.wait_ge(xT_mm, a.n + 1)
                    nc.scalar.copy(xcT[:, a.slot(2), :, :].rearrange("p c t -> p (c t)"), xT_ps).then_inc(xcT_sb, 1)
                    act.wait_ge(gate_mm, a.n + 1)
                    nc.scalar.copy(buT[:, :], bu_ps).then_inc(buT_sb, 1)
                if b.real:
                    act.wait_ge(nmax_s, b.n + 1)
                    nc.scalar.activation(aexp[:, :], sim_ps, ACT.Exp, bias=smax[:, 1:2], scale=1.0,
                                         accum_out=rsum[:, 0:1]).then_inc(aexp_sb, 1)
                if a.real:
                    wait(act, gated, a.n)
                    nc.scalar.activation(th[:, :], gate_ps, ACT.Tanh, scale=0.5).then_inc(th_sb, 1)
                if c.real:
                    act.wait_ge(x2T_mm, c.n + 1)
                    nc.scalar.copy(x2T[:, :, :].rearrange("p c t -> p (c t)"), x2T_ps).then_inc(x2T_sb, 1)
                if b.real:
                    act.wait_ge(aT_mm, b.n + 1)
                    nc.scalar.copy(aT[:, :], aT_ps)
                    nc.scalar.copy(vrow[:, :], vrow_ps).then_inc(aT_sb, 1)
                    act.wait_ge(nvmax_s, b.n + 1)
                    nc.scalar.activation(vrow[:, :], vrow[:, :], ACT.Exp, bias=vst[:, 1:2], scale=1.0,
                                         accum_out=vst[:, 2:3]).then_inc(vexp_sb, 1)
                    act.wait_ge(hq_mm, b.n + 1)
                    nc.scalar.copy(hqT[:, :, :].rearrange("p c t -> p (c t)"), hqT_ps).then_inc(hqT_sb, 1)
                if c.real:
                    act.wait_ge(g_mm, c.n + 1)
                    wait(act, hT_s, c.n)
                    nc.scalar.activation(thg[:, :], g_ps, ACT.Tanh, scale=0.5).then_inc(thg_sb, 1)
            run_pass1(act, step)

            act.wait_ge(wt_s, 1)
            nc.scalar.activation(top2[:, :, 1], top2[:, :, 1], ACT.Exp).then_inc(wexp_s, 1)

            def tiles(j, off):
                t, b = Seq(j, off, NTILES), Seq(j, off - 1, NTILES)
                c = Seq(j, off - 2, NTILES)
                if t.real:
                    act.wait_ge(tT_mm, t.n + 1)
                    nc.scalar.copy(x2T[:, :, :].rearrange("p c t -> p (c t)"), x2T_ps).then_inc(tT_sb, 1)
                if c.real:
                    act.wait_ge(ty_mm, c.n + 1)
                    wait(act, t_out[c.slot(2)], c.turn(2) * 16)
                    nc.scalar.activation(c_sb[:, c.slot(2), :], qv_ps, ACT.Copy, scale=0.5).then_inc(ty_sb, 1)
                if t.real:
                    act.wait_ge(tg_mm, t.n + 1)
                    wait(act, th_s, t.n)
                    nc.scalar.activation(thg[:, :], g_ps, ACT.Tanh, scale=0.5).then_inc(tth_s, 1)
                if b.real:
                    act.wait_ge(thT_mm, b.n + 1)
                    nc.scalar.copy(hT[:, :, :].rearrange("p c t -> p (c t)"), thT_ps).then_inc(thT_sb, 1)
            pipeline(act, tiles, NTILES, UNROLL, 2)

        @block.vector
        def _(dve):
            n = 1
            dve.wait_ge(setup, 1)
            nc.vector.tensor_scalar(decay[:, 2, :], decay[:, 1, :], 1.0, None, ALU.add).then_inc(setup, 1)
            dve.wait_ge(setup, 2)
            nc.vector.reciprocal(decay[:, 0, :], decay[:, 2, :]).then_inc(setup, 1)
            nc.vector.memset(apowT[:, :, 0:1], 1.0)
            dve.wait_ge(setup, 3)
            nc.vector.tensor_copy(apowT[:, :, 1], decay[:, 0, :]).then_inc(setup, 1)
            done, w = 4, 2
            while w < P:
                dve.wait_ge(setup, done)
                nc.vector.tensor_tensor(decay[:, 1, :], apowT[:, :, w - 1], decay[:, 0, :], ALU.mult).then_inc(setup, 1)
                dve.wait_ge(setup, done + 1)
                for c in range(DC):
                    last = nc.vector.tensor_scalar(apowT[:, c, w:2 * w], apowT[:, c, 0:w], decay[:, 1, c:c + 1], None, ALU.mult)
                last.then_inc(setup, 1)
                done, w = done + 2, 2 * w
            nc.vector.tensor_copy(tri_b[:, :], tri[:, :]).then_inc(pow_ready, 1)
            dve.wait_ge(apow_ps_ready, 1)
            nc.vector.tensor_scalar(apow[:, :], bp_ps, 0.5, None, ALU.mult).then_inc(apow_ready, 1)
            dve.wait_ge(apow_ready, 1)

            def norm_stats(t, src, bn, st_s, mv, mv_s, res_s):
                dve.wait_ge(res_s, t.n + 1)
                nc.vector.bn_stats(bn[:, :], src).then_inc(st_s, 1)
                wait_alone(dve, st_s, t.n + 1)
                nc.vector.bn_aggr(mv[:, :], bn[:, :]).then_inc(mv_s, 1)

            def norm_apply(t, dst, src, mv, rs, rs_s, out_sem):
                dve.wait_ge(rs_s, t.n + 1)
                nc.vector.tensor_scalar(dst, src, mv[:, 0:1], rs[:, 0:1], ALU.subtract, ALU.mult).then_inc(out_sem, 1)

            def step(j, off):
                a, b, c, d = (Seq(j, off - k) for k in range(4))
                if b.real:
                    dve.wait_ge(x1T_sb, b.n + 1)
                    for ch in range(DC):
                        last = nc.vector.tensor_scalar(qT[:, ch, :], x1T[:, ch, :], wsim_sb[:, 2, ch:ch + 1],
                                                       wsim_sb[:, 1, ch:ch + 1], ALU.mult, ALU.add)
                    last.then_inc(qT_sb, 1)
                if c.real:
                    dve.wait_ge(qv_mm, c.n + 1)
                    wait(dve, row_out[c.slot(2)], c.turn(2) * 32)
                    nc.vector.tensor_tensor(x2[:, c.slot(2), :], qv_ps, x1[:, c.slot(2), :], ALU.add).then_inc(res2, 1)
                    norm_stats(c, x2[:, c.slot(2), :], bn2, st2, mv2, mv2_s, res2)
                if b.real:
                    dve.wait_ge(sim_mm, b.n + 1)
                    nc.vector.reduce_max(smax[:, 0:1], sim_ps, AX_X).then_inc(smax_s, 1)
                    dve.wait_ge(smax_s, b.n + 1)
                    nc.vector.scalar_tensor_tensor(out=vcol[:, :], in0=smax[:, 0:1], scalar=bsim_sb[:, 0:1], in1=s_ps,
                                                   op0=ALU.add, op1=ALU.add).then_inc(v_s, 1)
                    nc.vector.tensor_scalar(smax[:, 1:2], smax[:, 0:1], -1.0, None, ALU.mult).then_inc(nmax_s, 1)
                if c.real:
                    norm_apply(c, x2[:, c.slot(2), :], x2[:, c.slot(2), :], mv2, rs2, rs2_s, x2_sb)
                if b.real:
                    dve.wait_ge(aexp_sb, b.n + 1)
                    nc.vector.reciprocal(rsum[:, 1:2], rsum[:, 0:1]).then_inc(rec_s, 1)
                    dve.wait_ge(rec_s, b.n + 1)
                    nc.vector.tensor_scalar(aexp[:, :], aexp[:, :], rsum[:, 1:2], None, ALU.mult).then_inc(anorm_s, 1)
                if d.real:
                    dve.wait_ge(y_mm, d.n + 1)
                    nc.vector.scalar_tensor_tensor(out=base[:, bass.ds(d.n, 1), :].rearrange("p a d -> p (a d)"), in0=y_ps,
                                                   scalar=0.5, in1=x2[:, d.slot(2), :], op0=ALU.mult, op1=ALU.add) \
                        .then_inc(base_s, 1)
                if b.real:
                    dve.wait_ge(aT_sb, b.n + 1)
                    nc.vector.reduce_max(vst[:, 0:1], vrow[:, :], AX_X).then_inc(vmax_s, 1)
                    dve.wait_ge(vmax_s, b.n + 1)
                    nc.vector.tensor_scalar(vst[:, 1:2], vst[:, 0:1], -1.0, None, ALU.mult).then_inc(nvmax_s, 1)
                if a.real:
                    dve.wait_ge(bp_mm, a.n + 1)
                    nc.vector.tensor_tensor(bpw[:, :], bp_ps, apow[:, :], ALU.mult).then_inc(bpw_sb, 1)
                if b.real:
                    dve.wait_ge(vexp_sb, b.n + 1)
                    nc.vector.reciprocal(vst[:, 3:4], vst[:, 2:3]).then_inc(vrec_s, 1)
                    dve.wait_ge(vrec_s, b.n + 1)
                    nc.vector.tensor_scalar(vprob[:, :], vrow[:, :], vst[:, 3:4], None, ALU.mult).then_inc(vprob_s, 1)
                if c.real:
                    dve.wait_ge(lg_mm, c.n + 1)
                    nc.vector.tensor_tensor(lg[:, :], lg_ps, ebias_sb[:, :], ALU.add).then_inc(lg_s, 1)
                    wait_alone(dve, lg_s, c.n + 1)
                    nc.vector.max(m8[:, :], lg[:, :]).then_inc(m8_s, 1)
                    wait_alone(dve, m8_s, c.n + 1)
                    nc.vector.max_index(i8[:, :], m8[:, :], lg[:, :]).then_inc(i8_s, 1)
                    nc.vector.tensor_copy(top2[:, bass.ds(c.n, 1), :].rearrange("p a k -> p (a k)"), m8[:, 0:TOPK])
                    dve.wait_ge(i8_s, c.n + 1)
                    nc.vector.tensor_copy(idxf[:, :], i8[:, 0:TOPK]).then_inc(idx_s, 1)
                    dve.wait_ge(idx_s, c.n + 1)
                    for k in range(TOPK):
                        last = nc.vector.tensor_scalar(oh[:, k, :], iota8[:, :], idxf[:, k:k + 1], None, ALU.is_equal)
                    last.then_inc(oh_s, 1)
                    dve.wait_ge(oh_s, c.n + 1)
                    nc.vector.tensor_tensor(ohb[:, :], oh[:, 0, :], oh[:, 1, :], ALU.add).then_inc(ohb_s, 1)
                if b.real:
                    dve.wait_ge(hqT_sb, b.n + 1)
                    nc.vector.tensor_tensor(x1hqT[:, :, :], x1T[:, :, :], hqT[:, :, :], ALU.mult).then_inc(x1hq_s, 1)
                if a.real:
                    dve.wait_ge(cum_mm, a.n + 1)
                    dve.wait_ge(th_sb, a.n + 1)
                    nc.vector.scalar_tensor_tensor(out=th[:, :], in0=th[:, :], scalar=1.0, in1=cum_ps,
                                                   op0=ALU.add, op1=ALU.mult).then_inc(gated, 1)
                    dve.wait_ge(gated, a.n + 1)
                    nc.vector.tensor_tensor(x1[:, a.slot(2), :], th[:, :], x_sb[:, a.slot(2), :], ALU.add).then_inc(res1, 1)
                    norm_stats(a, x1[:, a.slot(2), :], bn1, st1, mv1, mv1_s, res1)
                if c.real:
                    dve.wait_ge(thg_sb, c.n + 1)
                    nc.vector.scalar_tensor_tensor(out=thg[:, :], in0=thg[:, :], scalar=1.0, in1=g_ps,
                                                   op0=ALU.add, op1=ALU.mult).then_inc(hg_s, 1)
                if b.real:
                    dve.wait_ge(pb_mm, b.n + 1)
                    for ch in range(DC):
                        last = nc.vector.tensor_tensor_reduce(x1hcT[:, ch, :], x1T[:, ch, :], pb_ps, 1.0, 0.0, ALU.mult, ALU.add,
                                                              hc[:, ch:ch + 1])
                    last.then_inc(hc_s, 1)
                    dve.wait_ge(hc_s, b.n + 1)
                    for ch in range(DC):
                        last = nc.vector.tensor_scalar(x1hcT[:, ch, :], x1T[:, ch, :], hc[:, ch:ch + 1], None, ALU.mult)
                    last.then_inc(x1hc_s, 1)
                if a.real:
                    norm_apply(a, x1[:, a.slot(2), :], x1[:, a.slot(2), :], mv1, rs1, rs1_s, x1_sb)
                if c.real:
                    dve.wait_ge(u_mm, c.n + 1)
                    dve.wait_ge(hg_s, c.n + 1)
                    nc.vector.tensor_tensor(hT[:, :, :].rearrange("p c t -> p (c t)"), thg[:, :], u_ps, ALU.mult).then_inc(hT_s, 1)
                    dve.wait_ge(rank_mm, c.n + 1)
                    nc.vector.tensor_tensor(place[:, :], rank_ps, count[:, :], ALU.add).then_inc(place_s, 1)
                    dve.wait_ge(place_s, c.n + 1)
                    nc.vector.tensor_tensor(count[:, :], total_ps, count[:, :], ALU.add).then_inc(count_s, 1)
                    for k in range(TOPK):
                        last = nc.vector.tensor_tensor_reduce(junk8[:, k, :], oh[:, k, :], place[:, :], 1.0, 0.0, ALU.mult, ALU.add,
                                                              posf[:, k:k + 1])
                    last.then_inc(posf_s, 1)
                    dve.wait_ge(posf_s, c.n + 1)
                    nc.vector.tensor_copy(posall[:, bass.ds(c.n, 1), :].rearrange("p a k -> p (a k)"), posf[:, :])
                    nc.vector.tensor_copy(posr[:, c.slot(UNROLL), :], posf[:, :]).then_inc(pos_s, 1)
                    dve.wait_ge(count_s, c.n + 1)
            dve.wait_ge(const_in, 16 * NCONST)
            run_pass1(dve, step)

            dve.wait_ge(pos_s, NSEQ)
            nc.vector.tensor_scalar(padidx[:, :], count[:, :], iotap[:, 0:1], None, ALU.add).then_inc(pad_ready, 1)

            links = [0]

            def link(ins):
                links[0] += 1
                ins.then_inc(table, 1)
                dve.wait_ge(table, links[0])
            link(nc.vector.tensor_tensor(cnt1[:, :], count[:, :], ereg[:, :], ALU.subtract))
            link(nc.vector.tensor_scalar(cnti[:, :], cnt1[:, :], float(P - 1), None, ALU.add))
            link(nc.vector.tensor_scalar(cntsh[:, :], cnti[:, :], P.bit_length() - 1, None, ALU.arith_shift_right))
            link(nc.vector.tensor_copy(ntile[:, :], cntsh[:, :]))
            link(nc.vector.tensor_copy(tend[:, 0:1], ntile[:, 0:1]))
            for e in range(1, E):
                link(nc.vector.tensor_tensor(tend[:, e:e + 1], tend[:, e - 1:e], ntile[:, e:e + 1], ALU.add))
            link(nc.vector.tensor_scalar(skip[:, :], ntile[:, :], -float(P), float(REGION), ALU.mult, ALU.add))
            nc.vector.memset(tacc[:, 0, :], 0.0)
            link(nc.vector.tensor_scalar(tacc[:, 1, :], jrow[:, :], float(P), None, ALU.mult))
            for e in range(E):
                link(nc.vector.scalar_tensor_tensor(out=tacc[:, 0, :], in0=jrow[:, :], scalar=tend[0:1, e:e + 1],
                                                    in1=tacc[:, 0, :], op0=ALU.is_ge, op1=ALU.add))
                link(nc.vector.tensor_scalar(tacc[:, 2, :], jrow[:, :], tend[0:1, e:e + 1], skip[0:1, e:e + 1], ALU.is_ge, ALU.mult))
                link(nc.vector.tensor_tensor(tacc[:, 1, :], tacc[:, 1, :], tacc[:, 2, :], ALU.add))
            nc.vector.tensor_scalar(tile_e[:, :], tacc[:, 0, :], float(E - 1), None, ALU.min)
            nc.vector.tensor_copy(tile_row[:, :], tacc[:, 1, :]).then_inc(table_ready, 1)

            pos = posall[:, :, :].rearrange("p t k -> p (t k)")
            for e in range(E - 1, 0, -1):
                link(nc.vector.tensor_scalar(aexp[:, :], pos, float(e * REGION), skip[:, e - 1:e], ALU.is_ge, ALU.mult))
                link(nc.vector.tensor_tensor(pos, pos, aexp[:, :], ALU.subtract))
            nc.vector.engine_nop().then_inc(pos_final, 1)

            link(nc.vector.tensor_tensor(top2[:, :, 1], top2[:, :, 1], top2[:, :, 0], ALU.subtract))
            nc.vector.engine_nop().then_inc(wt_s, 1)
            dve.wait_ge(wexp_s, 1)
            link(nc.vector.tensor_scalar(top2[:, :, 0], top2[:, :, 1], 1.0, None, ALU.add))
            link(nc.vector.reciprocal(top2[:, :, 0], top2[:, :, 0]))
            link(nc.vector.tensor_tensor(top2[:, :, 1], top2[:, :, 1], top2[:, :, 0], ALU.mult))

            w2h = xcT[:, 0, :, :].rearrange("p c t -> p (c t)")

            def tiles(j, off):
                t = Seq(j, off, NTILES)
                if t.real:
                    dve.wait_ge(tth_s, t.n + 1)
                    nc.vector.scalar_tensor_tensor(out=thg[:, :], in0=thg[:, :], scalar=1.0, in1=g_ps,
                                                   op0=ALU.add, op1=ALU.mult).then_inc(thg_s, 1)
                    dve.wait_ge(tu_mm, t.n + 1)
                    dve.wait_ge(thg_s, t.n + 1)
                    wait(dve, thT_mm, t.n)
                    nc.vector.tensor_tensor(w2h[:, :], thg[:, :], u_ps, ALU.mult).then_inc(th_s, 1)
            pipeline(dve, tiles, NTILES, UNROLL, 0)

            def last_norm(j, off):
                t, b = Seq(j, off), Seq(j, off - 1)
                if t.real:
                    dve.wait_ge(ya_in[t.slot(2)], t.turn(2) * 16 + 16)
                    bt = base[:, bass.ds(t.n, 1), :].rearrange("p a d -> p (a d)")
                    nc.vector.scalar_tensor_tensor(out=th[:, :], in0=x_sb[:, t.slot(2), :],
                                                   scalar=top2[:, bass.ds(t.n, 1), 0], in1=bt,
                                                   op0=ALU.mult, op1=ALU.add).then_inc(acc_s, 1)
                    dve.wait_ge(acc_s, t.n + 1)
                    dve.wait_ge(yb_in[t.slot(2)], t.turn(2) * 16 + 16)
                if b.real:
                    wait(dve, out_done[b.slot(2)], b.turn(2) * 16)
                    norm_apply(b, x2[:, b.slot(2), :], x1[:, b.slot(2), :], mv1, rs1, rs3_s, out_s)
                if t.real:
                    nc.vector.scalar_tensor_tensor(out=x1[:, t.slot(2), :], in0=c_sb[:, t.slot(2), :],
                                                   scalar=top2[:, bass.ds(t.n, 1), 1], in1=th[:, :],
                                                   op0=ALU.mult, op1=ALU.add).then_inc(res3, 1)
                    wait(dve, out_s, t.n)
                    norm_stats(t, x1[:, t.slot(2), :], bn1, st3, mv1, mv3_s, res3)
            pipeline(dve, last_norm, NSEQ, UNROLL, 1)

        @block.tensor
        def _(pe):
            mm, tr = nc.tensor.matmul, nc.tensor.transpose
            pe.wait_ge(const_in, 16 * NCONST)
            pe.wait_ge(consts_ready, 4)
            pe.wait_ge(pow_ready, 1)
            for ch in range(DC):
                last = tr(bp_ps[:, ch * P:(ch + 1) * P], apowT[:, ch, :], ident[:, :])
            last.then_inc(apow_ps_ready, 1)
            pe.wait_ge(apow_ready, 1)

            def step(j, off):
                a, b, c, d = (Seq(j, off - k) for k in range(4))
                if b.real:
                    pe.wait_ge(x1_sb, b.n + 1)
                    wait(pe, hc_s, b.n)
                    for ch in range(DC):
                        last = tr(x1T_ps[:, ch * P:(ch + 1) * P], x1[:, b.slot(2), ch * P:(ch + 1) * P], ident[:, :])
                    last.then_inc(x1T_mm, 1)
                if a.real:
                    pe.wait_ge(x_in[a.slot(2)], a.turn(2) * 16 + 16)
                    pe.wait_ge(c_in[a.slot(2)], a.turn(2) * 16 + 16)
                    wait(pe, x2T_sb, a.n - 2)
                    wait(pe, xcT_sb, a.n)
                    for i, src in enumerate((x_sb, c_sb)):
                        for ch in range(DC):
                            last = tr(xT_ps[:, (i * DC + ch) * P:(i * DC + ch + 1) * P],
                                      src[:, a.slot(2), ch * P:(ch + 1) * P], ident[:, :])
                    last.then_inc(xT_mm, 1)

                def down(lo, hi):
                    for hch in range(lo, hi):
                        last = mm(y_ps, hT[:, hch, :], w2_sb[:, E - 1, hch, :], start=hch == 0, stop=hch == HC - 1)
                    if hi == HC:
                        last.then_inc(y_mm, 1)
                if d.real:
                    pe.wait_ge(hT_s, d.n + 1)
                    pe.wait_ge(hqT_sb, upto(d, 2))
                    wait(pe, base_s, d.n)
                    down(0, HC // 2)
                if b.real:
                    pe.wait_ge(qT_sb, b.n + 1)
                    pe.wait_ge(x1T_sb, b.n + 1)
                    wait(pe, count_s, b.n - 1)
                    wait(pe, aexp_sb, b.n)
                    for ch in range(DC):
                        mm(sim_ps, qT[:, ch, :], xcT[:, b.slot(2), DC + ch, :], start=ch == 0, stop=ch == DC - 1)
                    for ch in range(DC):
                        last = mm(s_ps, x1T[:, ch, :], wsim_sb[:, 0, ch:ch + 1], start=ch == 0, stop=ch == DC - 1)
                    last.then_inc(sim_mm, 1)
                if a.real:
                    pe.wait_ge(xcT_sb, a.n + 1)
                    wait(pe, gated, a.n)
                    for ch in range(DC):
                        mm(bu_ps, BwT_sb[:, ch, :], xcT[:, a.slot(2), ch, :], start=ch == 0, stop=ch == DC - 1)
                    for ch in range(DC):
                        mm(gate_ps, xcT[:, a.slot(2), ch, :], gwT_sb[:, ch, :], start=ch == 0, stop=False)
                    mm(gate_ps, ones_row[:, :], gb_sb[:, :], start=False, stop=True).then_inc(gate_mm, 1)
                if d.real:
                    down(HC // 2, HC)
                if c.real:
                    pe.wait_ge(x2_sb, c.n + 1)
                    pe.wait_ge(xcT_sb, upto(c, 3))
                    wait(pe, x2T_sb, c.n)
                    for ch in range(DC):
                        last = tr(x2T_ps[:, ch * P:(ch + 1) * P], x2[:, c.slot(2), ch * P:(ch + 1) * P], ident[:, :])
                    last.then_inc(x2T_mm, 1)
                if b.real:
                    pe.wait_ge(v_s, b.n + 1)
                    pe.wait_ge(anorm_s, b.n + 1)
                    pe.wait_ge(th_sb, upto(b, 2))
                    wait(pe, aT_sb, b.n)
                    tr(aT_ps, aexp[:, :], ident[:, :])
                    mm(vrow_ps, vcol[:, :], ident[:, :], start=True, stop=True).then_inc(aT_mm, 1)
                if a.real:
                    pe.wait_ge(buT_sb, a.n + 1)
                    wait(pe, x1T_sb, a.n)
                    mm(bp_ps, buT[:, :], CwT_sb[:, :], start=True, stop=True).then_inc(bp_mm, 1)

                def up(ps, w, lo, hi):
                    for hch in range(lo, hi):
                        for ch in range(DC):
                            last = mm(ps[:, hch * P:(hch + 1) * P], w13_sb[:, E - 1, ch, w * H + hch * P:w * H + (hch + 1) * P],
                                      x2T[:, ch, :], start=ch == 0, stop=ch == DC - 1)
                    return last
                if c.real:
                    pe.wait_ge(x2T_sb, c.n + 1)
                    pe.wait_ge(aexp_sb, upto(c, 2))
                    wait(pe, count_s, c.n)
                    for ch in range(DC):
                        last = mm(lg_ps, x2T[:, ch, :], rwT_sb[:, ch, :], start=ch == 0, stop=ch == DC - 1)
                    last.then_inc(lg_mm, 1)
                    if isinstance(c.n, int) and c.n == 0:
                        pe.wait_ge(last_in, 48)
                    wait(pe, hg_s, c.n)
                    up(g_ps, 0, 0, 2)
                if b.real:
                    pe.wait_ge(aT_sb, b.n + 1)
                    wait(pe, base_s, b.n - 1)
                    wait(pe, hqT_sb, b.n)
                    for ch in range(DC):
                        last = mm(hqT_ps[:, ch * P:(ch + 1) * P], c_sb[:, b.slot(2), ch * P:(ch + 1) * P], aT[:, :],
                                  start=True, stop=True)
                    last.then_inc(hq_mm, 1)
                if a.real:
                    pe.wait_ge(bpw_sb, a.n + 1)
                    wait(pe, aT_sb, a.n)
                    pe.wait_ge(th_sb, a.n + 1)
                    mm(cum_ps, tri[:, :], bpw[:, :], start=True, stop=True).then_inc(cum_mm, 1)
                if c.real:
                    up(g_ps, 0, 2, 4).then_inc(g_mm, 1)
                if b.real:
                    pe.wait_ge(vprob_s, b.n + 1)
                    pe.wait_ge(bpw_sb, upto(b, 2))
                    mm(pb_ps, ones_row[:, :], vprob[:, :], start=True, stop=True).then_inc(pb_mm, 1)
                if c.real:
                    wait(pe, hT_s, c.n)
                    up(u_ps, 1, 0, 2)
                    pe.wait_ge(ohb_s, c.n + 1)
                    mm(rank_ps, tri_b[:, :], ohb[:, :], start=True, stop=True)
                    mm(total_ps, ones_b[:, :], ohb[:, :], start=True, stop=True).then_inc(rank_mm, 1)
                    up(u_ps, 1, 2, 4).then_inc(u_mm, 1)
                if b.real:
                    wait(pe, res2, b.n)
                    mm(qv_ps, ones_row[:, :], bqv_sb[:, :], start=True, stop=False)
                    for g, (feat, ready) in enumerate(((x1T, x1T_sb), (hqT, hqT_sb), (x1hqT, x1hq_s), (x1hcT, x1hc_s))):
                        pe.wait_ge(ready, b.n + 1)
                        for ch in range(DC):
                            last = mm(qv_ps, feat[:, ch, :], Wqv_sb[:, g * DC + ch, :], start=False,
                                      stop=g == 3 and ch == DC - 1)
                    last.then_inc(qv_mm, 1)
            run_pass1(pe, step)

            pe.wait_ge(table_ready, 1)
            pe.wait_ge(moe_in, 16 * 3 * (E - 1))
            pe.wait_ge(last_in, 96)

            def tiles(j, off):
                t, b, c = (Seq(j, off - k, NTILES) for k in range(3))
                if t.real:
                    pe.wait_ge(t_in[t.slot(2)], t.turn(2) * 16 + 16)
                    wait(pe, tT_sb, t.n)
                    for ch in range(DC):
                        last = tr(x2T_ps[:, ch * P:(ch + 1) * P], x_sb[:, t.slot(2), ch * P:(ch + 1) * P], ident[:, :])
                    last.then_inc(tT_mm, 1)
                if c.real:
                    ec = pe.value_load(tile_e[0:1, bass.ds(c.n, 1)], min_val=0, max_val=E - 1)
                    pe.wait_ge(thT_sb, c.n + 1)
                    wait(pe, ty_sb, c.n)
                    for hch in range(HC):
                        last = mm(qv_ps, hT[:, hch, :], w2_sb[:, bass.ds(ec, 1), hch, :].rearrange("p a n -> p (a n)"),
                                  start=hch == 0, stop=hch == HC - 1)
                    last.then_inc(ty_mm, 1)
                if t.real:
                    e = pe.value_load(tile_e[0:1, bass.ds(t.n, 1)], min_val=0, max_val=E - 1)
                    pe.wait_ge(tT_sb, t.n + 1)
                    wait(pe, thg_s, t.n)
                    for ch in range(DC):
                        last = mm(g_ps, x2T[:, ch, :], w13_sb[:, bass.ds(e, 1), ch, 0:H].rearrange("p a n -> p (a n)"),
                                  start=ch == 0, stop=ch == DC - 1)
                    last.then_inc(tg_mm, 1)
                if b.real:
                    pe.wait_ge(th_s, b.n + 1)
                    wait(pe, thT_sb, b.n)
                    for hch in range(HC):
                        last = tr(thT_ps[:, hch * P:(hch + 1) * P], xcT[:, 0, hch, :], ident[:, :])
                    last.then_inc(thT_mm, 1)
                if t.real:
                    wait(pe, th_s, t.n)
                    for ch in range(DC):
                        last = mm(u_ps, x2T[:, ch, :], w13_sb[:, bass.ds(e, 1), ch, H:2 * H].rearrange("p a n -> p (a n)"),
                                  start=ch == 0, stop=ch == DC - 1)
                    last.then_inc(tu_mm, 1)
            pipeline(pe, tiles, NTILES, UNROLL, 2)


def kernel(x, ctx_1024, L0_attn_B_w, L0_attn_C_w, L0_attn_gate_w, L0_attn_gate_b, L0_attn_log_decay,
           L0_xattn_w_sim, L0_xattn_b_sim, L0_xattn_W_qv, L0_xattn_b_qv, L0_ffn_router_w, L0_ffn_experts_bias,
           L0_ffn_w1, L0_ffn_w3, L0_ffn_w2, L0_ffn_sw1, L0_ffn_sw3, L0_ffn_sw2):
    import concourse.bacc as bacc
    from concourse.bass_utils import run_bass_kernel_spmd

    def lay(a):
        return np.ascontiguousarray(a)
    arrays = {
        "x": lay(x), "ctxt": lay(ctx_1024),
        "BwT": lay(np.asarray(L0_attn_B_w).T), "CwT": lay(np.asarray(L0_attn_C_w).T),
        "gwT": lay(np.asarray(L0_attn_gate_w).T), "gate_b": lay(L0_attn_gate_b).reshape(1, D),
        "log_decay": lay(np.asarray(L0_attn_log_decay).reshape(DC, P).T),
        "w_sim": lay(np.asarray(L0_xattn_w_sim).reshape(3, DC, P).transpose(2, 0, 1)),
        "b_sim": lay(L0_xattn_b_sim), "W_qv": lay(L0_xattn_W_qv), "b_qv": lay(L0_xattn_b_qv).reshape(1, D),
        "rwT": lay(np.asarray(L0_ffn_router_w).T), "ebias": lay(L0_ffn_experts_bias),
        "w1": lay(L0_ffn_w1), "w3": lay(L0_ffn_w3), "w2": lay(L0_ffn_w2),
        "sw1": lay(L0_ffn_sw1).reshape(D, H), "sw3": lay(L0_ffn_sw3).reshape(D, H), "sw2": lay(L0_ffn_sw2).reshape(H, D),
        "c_ident": np.eye(P, dtype=np.float32), "c_tri": np.triu(np.ones((P, P), np.float32), 1),
        "c_iota8": np.tile(np.arange(E, dtype=np.float32), (P, 1)),
        "c_iotap": np.arange(P, dtype=np.float32).reshape(P, 1),
        "c_jrow": np.arange(NTILES, dtype=np.float32).reshape(1, NTILES),
        "c_ereg": (np.arange(E, dtype=np.float32) * REGION).reshape(1, E),
    }
    nc = bacc.Bacc("TRN2", target_bir_lowering=False, num_devices=1)
    args = [nc.dram_tensor(f"in_{k}", a.shape, mybir.dt.from_np(a.dtype), kind="ExternalInput").ap()
            for k, a in arrays.items()]
    args.append(nc.dram_tensor("out_0", (NSEQ, L, D), F32, kind="ExternalOutput").ap())
    args.append(nc.dram_tensor("expert_rows", (ROWS, D), F32, kind="Internal").ap())
    args.append(nc.dram_tensor("expert_out", (NTILES, P, D), F32, kind="Internal").ap())
    build(nc, *args)
    r = run_bass_kernel_spmd(nc, [{f"in_{k}": a for k, a in arrays.items()}], core_ids=[0])
    return r.results[0]["out_0"]
```
